# Optimizing a Trainium2 kernel written in Bass

```python
import numpy as np
import jax
import jax.numpy as jnp

def _softmax(x, axis=-1):
    return jax.nn.softmax(x, axis=axis)

def _gelu(x):
    return jax.nn.gelu(x, approximate=True)

def _silu(x):
    return jax.nn.silu(x)

def _sigmoid(x):
    return jax.nn.sigmoid(x)

def _layernorm(x, axis=-1, eps=1e-05):
    m = jnp.mean(x, axis=axis, keepdims=True)
    v = jnp.var(x, axis=axis, keepdims=True)
    return (x - m) / jnp.sqrt(v + eps)

def _scatter_add(tgt, idx, src, axis=0):
    return tgt.at[idx].add(src)

def _segment_sum(src, seg, n):
    return jax.ops.segment_sum(src, seg, n)
kernel_name = 'mk_xattn_seq_d4_seqx_r4_cd2310'

def setup_inputs(seed: int=0):
    np.random.seed(seed)
    _w = jnp.asarray

    def _rec_inputs():
        import jax
        import jax.numpy as jnp
        _rk = jax.random.key(seed)
        x = -0.000125 + 0.9999 * jax.random.normal(jax.random.fold_in(_rk, 1), (4, 512, 256), jnp.float32)
        _lenS = 512 - jax.random.randint(jax.random.fold_in(_rk, 7), (4,), 0, max(1, 512 // 4) + 1, jnp.int32)
        _lenS2 = 1024 - jax.random.randint(jax.random.fold_in(_rk, 8), (4,), 0, max(1, 1024 // 4) + 1, jnp.int32)
        _ctx_2048P = jax.random.normal(jax.random.fold_in(_rk, 11), (4, 16, 512), jnp.float32)
        _ctx_2048c = jax.random.dirichlet(jax.random.fold_in(_rk, 511), 0.3 * jnp.ones((16,), jnp.float32), (4, 1024))
        _ctx_2048t = jnp.einsum('bsk,bkd->bsd', _ctx_2048c, _ctx_2048P)
        _ctx_2048t = _ctx_2048t * jax.lax.rsqrt(jnp.mean(jnp.square(_ctx_2048t)) + 1e-12) * 0.953939
        ctx_2048 = 5.36139e-06 + 1.00015 * (_ctx_2048t + 0.3 * jax.random.normal(jax.random.fold_in(_rk, 611), (4, 1024, 512), jnp.float32))
        _validS = jnp.arange(512)[None, :] < _lenS[:, None]
        _validS2 = jnp.arange(1024)[None, :] < _lenS2[:, None]
        _causal = jnp.tril(jnp.ones((512, 512), dtype=bool))
        mask_S_fk1 = jnp.where(_validS[0], 1.0, 0.0).astype(jnp.float32)
        mask_S_fk0 = jnp.where(_validS[0], 0.0, 1.0).astype(jnp.float32)
        return (x, ctx_2048, mask_S_fk1, mask_S_fk0)
    x, ctx_2048, mask_S_fk1, mask_S_fk0 = _rec_inputs()

    def _L0_xattn_setup():
        import jax, jax.numpy as jnp
        import numpy as np
        HEADS = 16
        HEAD_DIM = 64
        SUPPRESS = 20.0
        key = jax.random.key(seed)
        ks = jax.random.split(key, 8)
        B, HW, C, T, CT = (8, 1024, 256, 77, 512)
        inner = HEADS * HEAD_DIM
        scale = 0.02
        return {'hidden_states': jax.random.normal(ks[0], (B, HW, C), jnp.float32), 'encoder_hidden_states': jax.random.normal(ks[1], (B, T, CT), jnp.float32), 'mask_A': (jax.random.uniform(ks[2], (HW,)) > 0.5).astype(jnp.float32), 'mask_B': (jax.random.uniform(ks[3], (HW,)) > 0.5).astype(jnp.float32), 'Wq': jax.random.normal(ks[4], (C, inner), jnp.float32) * scale, 'Wk': jax.random.normal(ks[5], (CT, inner), jnp.float32) * scale, 'Wv': jax.random.normal(ks[6], (CT, inner), jnp.float32) * scale, 'Wo': jax.random.normal(ks[7], (inner, C), jnp.float32) * scale, 'bo': jnp.zeros((C,), jnp.float32), 'token_indices_A': jnp.array([2, 3], dtype=jnp.int64), 'token_indices_B': jnp.array([5, 6], dtype=jnp.int64)}
    _L0_xattn_all = _L0_xattn_setup()
    _L0_xattn_in = {k: v for k, v in _L0_xattn_all.items() if k in ('Wq', 'Wk', 'Wv', 'Wo', 'bo', 'token_indices_A', 'token_indices_B')}
    del _L0_xattn_all

    def _L1_xattn_setup():
        import jax, jax.numpy as jnp
        import numpy as np
        D_MODEL = 256
        N_HEADS = 16
        N_KV_HEADS = 4
        HEAD_DIM = D_MODEL // N_HEADS
        SPEAKER_DIM = 512
        EPS = 1e-05

        def rmsnorm(x, w, eps=EPS):
            xf = x.astype(jnp.float32)
            inv = jax.lax.rsqrt(jnp.mean(xf * xf, axis=-1, keepdims=True) + eps)
            return (xf * inv).astype(x.dtype) * w
        key = jax.random.key(seed)
        ks = jax.random.split(key, 7)
        B, T, S = (4, 512, 128)
        x = jax.random.normal(ks[0], (B, T, D_MODEL), dtype=jnp.float32)
        cond = jax.random.normal(ks[1], (B, S, SPEAKER_DIM), dtype=jnp.float32)
        sq = 0.02
        wq = jax.random.normal(ks[2], (D_MODEL, N_HEADS * HEAD_DIM), dtype=jnp.float32) * sq
        wk = jax.random.normal(ks[3], (SPEAKER_DIM, N_KV_HEADS * HEAD_DIM), dtype=jnp.float32) * sq
        wv = jax.random.normal(ks[4], (SPEAKER_DIM, N_KV_HEADS * HEAD_DIM), dtype=jnp.float32) * sq
        wo = jax.random.normal(ks[5], (N_HEADS * HEAD_DIM, D_MODEL), dtype=jnp.float32) * sq
        norm_w = jnp.ones((D_MODEL,), dtype=jnp.float32)
        return {'x': x, 'cond': cond, 'wq': wq, 'wk': wk, 'wv': wv, 'wo': wo, 'norm_w': norm_w}
    _L1_xattn_all = _L1_xattn_setup()
    _L1_xattn_in = {k: v for k, v in _L1_xattn_all.items() if k in ('wq', 'wk', 'wv', 'wo', 'norm_w')}
    del _L1_xattn_all

    def _L2_xattn_setup():
        import jax, jax.numpy as jnp
        import numpy as np
        HEADS = 16
        HEAD_DIM = 64
        SUPPRESS = 20.0
        key = jax.random.key(seed)
        ks = jax.random.split(key, 8)
        B, HW, C, T, CT = (8, 1024, 256, 77, 512)
        inner = HEADS * HEAD_DIM
        scale = 0.02
        return {'hidden_states': jax.random.normal(ks[0], (B, HW, C), jnp.float32), 'encoder_hidden_states': jax.random.normal(ks[1], (B, T, CT), jnp.float32), 'mask_A': (jax.random.uniform(ks[2], (HW,)) > 0.5).astype(jnp.float32), 'mask_B': (jax.random.uniform(ks[3], (HW,)) > 0.5).astype(jnp.float32), 'Wq': jax.random.normal(ks[4], (C, inner), jnp.float32) * scale, 'Wk': jax.random.normal(ks[5], (CT, inner), jnp.float32) * scale, 'Wv': jax.random.normal(ks[6], (CT, inner), jnp.float32) * scale, 'Wo': jax.random.normal(ks[7], (inner, C), jnp.float32) * scale, 'bo': jnp.zeros((C,), jnp.float32), 'token_indices_A': jnp.array([2, 3], dtype=jnp.int64), 'token_indices_B': jnp.array([5, 6], dtype=jnp.int64)}
    _L2_xattn_all = _L2_xattn_setup()
    _L2_xattn_in = {k: v for k, v in _L2_xattn_all.items() if k in ('Wq', 'Wk', 'Wv', 'Wo', 'bo', 'token_indices_A', 'token_indices_B')}
    del _L2_xattn_all

    def _L3_xattn_setup():
        import jax, jax.numpy as jnp
        import numpy as np
        HEADS = 16
        HEAD_DIM = 64
        SUPPRESS = 20.0
        key = jax.random.key(seed)
        ks = jax.random.split(key, 8)
        B, HW, C, T, CT = (8, 1024, 256, 77, 512)
        inner = HEADS * HEAD_DIM
        scale = 0.02
        return {'hidden_states': jax.random.normal(ks[0], (B, HW, C), jnp.float32), 'encoder_hidden_states': jax.random.normal(ks[1], (B, T, CT), jnp.float32), 'mask_A': (jax.random.uniform(ks[2], (HW,)) > 0.5).astype(jnp.float32), 'mask_B': (jax.random.uniform(ks[3], (HW,)) > 0.5).astype(jnp.float32), 'Wq': jax.random.normal(ks[4], (C, inner), jnp.float32) * scale, 'Wk': jax.random.normal(ks[5], (CT, inner), jnp.float32) * scale, 'Wv': jax.random.normal(ks[6], (CT, inner), jnp.float32) * scale, 'Wo': jax.random.normal(ks[7], (inner, C), jnp.float32) * scale, 'bo': jnp.zeros((C,), jnp.float32), 'token_indices_A': jnp.array([2, 3], dtype=jnp.int64), 'token_indices_B': jnp.array([5, 6], dtype=jnp.int64)}
    _L3_xattn_all = _L3_xattn_setup()
    _L3_xattn_in = {k: v for k, v in _L3_xattn_all.items() if k in ('Wq', 'Wk', 'Wv', 'Wo', 'bo', 'token_indices_A', 'token_indices_B')}
    del _L3_xattn_all
    return {'x': x, 'ctx_2048': ctx_2048, 'mask_S_fk1': mask_S_fk1, 'mask_S_fk0': mask_S_fk0, 'L0_xattn_Wq': _L0_xattn_in['Wq'], 'L0_xattn_Wk': _L0_xattn_in['Wk'], 'L0_xattn_Wv': _L0_xattn_in['Wv'], 'L0_xattn_Wo': _L0_xattn_in['Wo'], 'L0_xattn_bo': _L0_xattn_in['bo'], 'L0_xattn_token_indices_A': _L0_xattn_in['token_indices_A'], 'L0_xattn_token_indices_B': _L0_xattn_in['token_indices_B'], 'L1_xattn_wq': _L1_xattn_in['wq'], 'L1_xattn_wk': _L1_xattn_in['wk'], 'L1_xattn_wv': _L1_xattn_in['wv'], 'L1_xattn_wo': _L1_xattn_in['wo'], 'L1_xattn_norm_w': _L1_xattn_in['norm_w'], 'L2_xattn_Wq': _L2_xattn_in['Wq'], 'L2_xattn_Wk': _L2_xattn_in['Wk'], 'L2_xattn_Wv': _L2_xattn_in['Wv'], 'L2_xattn_Wo': _L2_xattn_in['Wo'], 'L2_xattn_bo': _L2_xattn_in['bo'], 'L2_xattn_token_indices_A': _L2_xattn_in['token_indices_A'], 'L2_xattn_token_indices_B': _L2_xattn_in['token_indices_B'], 'L3_xattn_Wq': _L3_xattn_in['Wq'], 'L3_xattn_Wk': _L3_xattn_in['Wk'], 'L3_xattn_Wv': _L3_xattn_in['Wv'], 'L3_xattn_Wo': _L3_xattn_in['Wo'], 'L3_xattn_bo': _L3_xattn_in['bo'], 'L3_xattn_token_indices_A': _L3_xattn_in['token_indices_A'], 'L3_xattn_token_indices_B': _L3_xattn_in['token_indices_B']}

def reference(x, ctx_2048, mask_S_fk1, mask_S_fk0, L0_xattn_Wq, L0_xattn_Wk, L0_xattn_Wv, L0_xattn_Wo, L0_xattn_bo, L0_xattn_token_indices_A, L0_xattn_token_indices_B, L1_xattn_wq, L1_xattn_wk, L1_xattn_wv, L1_xattn_wo, L1_xattn_norm_w, L2_xattn_Wq, L2_xattn_Wk, L2_xattn_Wv, L2_xattn_Wo, L2_xattn_bo, L2_xattn_token_indices_A, L2_xattn_token_indices_B, L3_xattn_Wq, L3_xattn_Wk, L3_xattn_Wv, L3_xattn_Wo, L3_xattn_bo, L3_xattn_token_indices_A, L3_xattn_token_indices_B):
    import jax
    import jax.numpy as jnp

    def _L0_xattn_ref(hidden_states, encoder_hidden_states, mask_A, mask_B, Wq, Wk, Wv, Wo, bo, token_indices_A, token_indices_B):
        import jax, jax.numpy as jnp
        import numpy as np
        HEADS = 16
        HEAD_DIM = 64
        SUPPRESS = 20.0
        B, HW, C = hidden_states.shape
        T = encoder_hidden_states.shape[1]
        residual = hidden_states
        q = hidden_states @ Wq
        k = encoder_hidden_states @ Wk
        v = encoder_hidden_states @ Wv
        q = q.reshape(B, HW, HEADS, HEAD_DIM).transpose(0, 2, 1, 3)
        k = k.reshape(B, T, HEADS, HEAD_DIM).transpose(0, 2, 1, 3)
        v = v.reshape(B, T, HEADS, HEAD_DIM).transpose(0, 2, 1, 3)
        scale = HEAD_DIM ** (-0.5)
        logits = jnp.einsum('bhqd,bhkd->bhqk', q, k) * scale
        suppress_A_in = 1.0 - mask_A
        suppress_B_in = 1.0 - mask_B
        col_bias = jnp.zeros((HW, T), logits.dtype)
        col_bias = col_bias.at[:, token_indices_A].set((-SUPPRESS * suppress_A_in)[:, None])
        col_bias = col_bias.at[:, token_indices_B].set((-SUPPRESS * suppress_B_in)[:, None])
        logits = logits + col_bias[None, None, :, :]
        probs = jax.nn.softmax(logits, axis=-1)
        out = jnp.einsum('bhqk,bhkd->bhqd', probs, v)
        out = out.transpose(0, 2, 1, 3).reshape(B, HW, HEADS * HEAD_DIM)
        out = out @ Wo + bo
        out = out + residual
        return out

    def _L1_xattn_ref(x, cond, wq, wk, wv, wo, norm_w):
        import jax, jax.numpy as jnp
        import numpy as np
        D_MODEL = 256
        N_HEADS = 16
        N_KV_HEADS = 4
        HEAD_DIM = D_MODEL // N_HEADS
        SPEAKER_DIM = 512
        EPS = 1e-05

        def rmsnorm(x, w, eps=EPS):
            xf = x.astype(jnp.float32)
            inv = jax.lax.rsqrt(jnp.mean(xf * xf, axis=-1, keepdims=True) + eps)
            return (xf * inv).astype(x.dtype) * w
        B, T, _ = x.shape
        S = cond.shape[1]
        n_rep = N_HEADS // N_KV_HEADS
        residual = x
        xn = rmsnorm(x, norm_w)
        q = (xn @ wq).reshape(B, T, N_HEADS, HEAD_DIM)
        k = (cond @ wk).reshape(B, S, N_KV_HEADS, HEAD_DIM)
        v = (cond @ wv).reshape(B, S, N_KV_HEADS, HEAD_DIM)
        qg = q.reshape(B, T, N_KV_HEADS, n_rep, HEAD_DIM)
        scale = 1.0 / np.sqrt(HEAD_DIM).astype(np.float32)
        scores = jnp.einsum('btgrd,bsgd->bgrts', qg, k) * scale
        attn = jax.nn.softmax(scores.astype(jnp.float32), axis=-1).astype(q.dtype)
        out = jnp.einsum('bgrts,bsgd->btgrd', attn, v).reshape(B, T, N_HEADS * HEAD_DIM)
        return residual + out @ wo

    def _L2_xattn_ref(hidden_states, encoder_hidden_states, mask_A, mask_B, Wq, Wk, Wv, Wo, bo, token_indices_A, token_indices_B):
        import jax, jax.numpy as jnp
        import numpy as np
        HEADS = 16
        HEAD_DIM = 64
        SUPPRESS = 20.0
        B, HW, C = hidden_states.shape
        T = encoder_hidden_states.shape[1]
        residual = hidden_states
        q = hidden_states @ Wq
        k = encoder_hidden_states @ Wk
        v = encoder_hidden_states @ Wv
        q = q.reshape(B, HW, HEADS, HEAD_DIM).transpose(0, 2, 1, 3)
        k = k.reshape(B, T, HEADS, HEAD_DIM).transpose(0, 2, 1, 3)
        v = v.reshape(B, T, HEADS, HEAD_DIM).transpose(0, 2, 1, 3)
        scale = HEAD_DIM ** (-0.5)
        logits = jnp.einsum('bhqd,bhkd->bhqk', q, k) * scale
        suppress_A_in = 1.0 - mask_A
        suppress_B_in = 1.0 - mask_B
        col_bias = jnp.zeros((HW, T), logits.dtype)
        col_bias = col_bias.at[:, token_indices_A].set((-SUPPRESS * suppress_A_in)[:, None])
        col_bias = col_bias.at[:, token_indices_B].set((-SUPPRESS * suppress_B_in)[:, None])
        logits = logits + col_bias[None, None, :, :]
        probs = jax.nn.softmax(logits, axis=-1)
        out = jnp.einsum('bhqk,bhkd->bhqd', probs, v)
        out = out.transpose(0, 2, 1, 3).reshape(B, HW, HEADS * HEAD_DIM)
        out = out @ Wo + bo
        out = out + residual
        return out

    def _L3_xattn_ref(hidden_states, encoder_hidden_states, mask_A, mask_B, Wq, Wk, Wv, Wo, bo, token_indices_A, token_indices_B):
        import jax, jax.numpy as jnp
        import numpy as np
        HEADS = 16
        HEAD_DIM = 64
        SUPPRESS = 20.0
        B, HW, C = hidden_states.shape
        T = encoder_hidden_states.shape[1]
        residual = hidden_states
        q = hidden_states @ Wq
        k = encoder_hidden_states @ Wk
        v = encoder_hidden_states @ Wv
        q = q.reshape(B, HW, HEADS, HEAD_DIM).transpose(0, 2, 1, 3)
        k = k.reshape(B, T, HEADS, HEAD_DIM).transpose(0, 2, 1, 3)
        v = v.reshape(B, T, HEADS, HEAD_DIM).transpose(0, 2, 1, 3)
        scale = HEAD_DIM ** (-0.5)
        logits = jnp.einsum('bhqd,bhkd->bhqk', q, k) * scale
        suppress_A_in = 1.0 - mask_A
        suppress_B_in = 1.0 - mask_B
        col_bias = jnp.zeros((HW, T), logits.dtype)
        col_bias = col_bias.at[:, token_indices_A].set((-SUPPRESS * suppress_A_in)[:, None])
        col_bias = col_bias.at[:, token_indices_B].set((-SUPPRESS * suppress_B_in)[:, None])
        logits = logits + col_bias[None, None, :, :]
        probs = jax.nn.softmax(logits, axis=-1)
        out = jnp.einsum('bhqk,bhkd->bhqd', probs, v)
        out = out.transpose(0, 2, 1, 3).reshape(B, HW, HEADS * HEAD_DIM)
        out = out @ Wo + bo
        out = out + residual
        return out
    x = _L0_xattn_ref(x, ctx_2048, mask_S_fk1, mask_S_fk0, L0_xattn_Wq, L0_xattn_Wk, L0_xattn_Wv, L0_xattn_Wo, L0_xattn_bo, L0_xattn_token_indices_A, L0_xattn_token_indices_B)
    x = _L1_xattn_ref(x, ctx_2048, L1_xattn_wq, L1_xattn_wk, L1_xattn_wv, L1_xattn_wo, L1_xattn_norm_w)
    x = _L2_xattn_ref(x, ctx_2048, mask_S_fk1, mask_S_fk0, L2_xattn_Wq, L2_xattn_Wk, L2_xattn_Wv, L2_xattn_Wo, L2_xattn_bo, L2_xattn_token_indices_A, L2_xattn_token_indices_B)
    x = _L3_xattn_ref(x, ctx_2048, mask_S_fk1, mask_S_fk0, L3_xattn_Wq, L3_xattn_Wk, L3_xattn_Wv, L3_xattn_Wo, L3_xattn_bo, L3_xattn_token_indices_A, L3_xattn_token_indices_B)
    return x

_drawn_inputs = setup_inputs


def setup_inputs(seed=0):
    import zlib

    import numpy as np

    out = dict(_drawn_inputs(seed))
    spreads = {'L0_xattn_bo': (0.0, 0.1),
     'L1_xattn_norm_w': (1.0, 0.6),
     'L2_xattn_bo': (0.0, 0.1),
     'L3_xattn_bo': (0.0, 0.1)}
    factors = {'mask_S_fk1': 8.0,
     'mask_S_fk0': 8.0,
     'L0_xattn_Wq': 8.0,
     'L0_xattn_Wk': 8.0,
     'L1_xattn_wq': 8.0,
     'L1_xattn_wk': 8.0,
     'L2_xattn_Wq': 8.0,
     'L2_xattn_Wk': 8.0,
     'L3_xattn_Wq': 8.0,
     'L3_xattn_Wk': 8.0}
    for name, (base, spread) in spreads.items():
        noise = np.random.default_rng([zlib.crc32(name.encode()), seed]).standard_normal(out[name].shape)
        drawn = base * np.exp(spread * noise) if base else spread * noise
        out[name] = jnp.asarray(drawn.astype(out[name].dtype))
    for name, factor in factors.items():
        out[name] = (out[name] * factor).astype(out[name].dtype)
    return out
```

```python
from contextlib import ExitStack

import concourse.bass as bass
from concourse import mybir

ALU = mybir.AluOpType
ACT = mybir.ActivationFunctionType
F32 = mybir.dt.float32
F16 = mybir.dt.float16
I32 = mybir.dt.int32
AX_X = mybir.AxisListType.X

P = 128
B, TQ, C = 4, 512, 256
TK, CT = 1024, 512
CQ, CK, KT, QT = C // P, CT // P, TK // P, TQ // P
HEADS, HD = 16, 64
PAIRS = HEADS // 2
GROUPS, REP, GD, GP = 4, 4, 16, 32
HALF = TQ // 2
STEPS = B * PAIRS
UNITS = 8
BANK = 512
SUPPRESS = 20.0
EPS = 1e-5
WS = 64.0
VS = 16.0
QS = HD ** -0.5 / WS
GQS = GD ** -0.5 / WS
WQ0, WK0, WV0 = 0, CQ * P, (CQ + CK) * P
WCOLS = WV0 + CK * P
GCOLS = P + 2 * CK * GD
WIDE = (0, 2, 3)
N_CONST = 7
FLAG_Q, FLAG_K, FLAG_LO, FLAG_A = range(4)
LIKE = 10
PV_AT = {4: range(0, 2), 5: range(2, 4), 6: range(4, 5), 7: range(5, 8)}


def reaches(eng, sem, value):
    if isinstance(value, int) and value <= 0:
        return
    eng.wait_ge(sem, value)


def run_steps(eng, step):
    step(0, 0, 0)
    step(1, 1, 0)
    with eng.Fori(1, STEPS // 2 - 1) as g:
        step(g * 2, LIKE, g)
        step(g * 2 + 1, LIKE + 1, g)
    step(STEPS - 2, STEPS - 2, STEPS // 2 - 1)
    step(STEPS - 1, STEPS - 1, STEPS // 2 - 1)
    step(STEPS, STEPS, STEPS // 2)


def batch_of(p):
    return p // PAIRS if isinstance(p, int) else (p >> 3).with_bounds(min_val=0, max_val=B - 1)


def xs_count(layer, q):
    return batch_of(q) + (B * layer + 1)


def ctx_count(layer, q, half):
    return batch_of(q) * 2 + (2 * B * layer + half + 1)


def build(nc, a, out):
    with ExitStack() as ctx:
        def sb(name, shape, dt):
            return ctx.enter_context(nc.sbuf_tensor(name, shape, dt))

        def sem(name):
            return ctx.enter_context(nc.semaphore(name))

        x32 = sb("x32", [P, CQ, B * TQ], F32)
        xh = sb("xh", [P, CQ, TQ], F16)
        xl = sb("xl", [P, CQ, TQ], F16)
        xn32 = sb("xn32", [P, CQ, TQ], F32)
        inv_rms = sb("inv_rms", [P, B * TQ], F32)
        ctx_raw = sb("ctx_raw", [P, CK, BANK], F32)
        ctx_h = sb("ctx_h", [P, 2, CK, BANK], F16)
        ctx_l = sb("ctx_l", [P, 2, CK, BANK], F16)
        w_raw = sb("w_raw", [P, WCOLS], F32)
        w_h = sb("w_h", [P, 2, WCOLS], F16)
        w_l = sb("w_l", [P, 2, WCOLS], F16)
        wo_raw = sb("wo_raw", [P, C], F32)
        wo_h = sb("wo_h", [P, C], F16)
        wo_l = sb("wo_l", [P, C], F16)
        kk = sb("kk", [P, 2, 2, TK], F16)
        k2 = sb("k2", [P, 2, 2, TK], F16)
        qq = sb("qq", [P, 2, 2, TQ], F16)
        q2 = sb("q2", [P, 2, 2, TQ], F16)
        v_new = sb("v_new", [P, KT, P], F32)
        v32 = sb("v32", [P, 2, KT, P], F32)
        prob = sb("prob", [P, 4, TK], F32)
        pt = sb("pt", [P, 2, 2 * KT * TQ], F32)
        o_h = sb("o_h", [P, TQ], F16)
        o_l = sb("o_l", [P, TQ], F16)
        negmax = sb("negmax", [P, 4], F32)
        rsum = sb("rsum", [P, 4], F32)
        rinv = sb("rinv", [P, 4], F32)
        ident = sb("ident_sb", [P, P], F32)
        ones = sb("ones_sb", [P, P], F32)
        flags = sb("flags_sb", [P, 4], F32)
        bo = sb("bo_sb", [P, 3 * CQ], F32)
        norm_w = sb("norm_w_sb", [P, CQ], F32)
        gw_h = sb("gw_h", [P, GCOLS], F16)
        gw_l = sb("gw_l", [P, GCOLS], F16)
        gq_h = sb("gq_h", [P, CQ, REP, 4, GP], F16)
        gq_l = sb("gq_l", [P, CQ, REP, 4, GP], F16)
        gk_h = sb("gk_h", [P, CK, 4, GP], F16)
        gk_l = sb("gk_l", [P, CK, 4, GP], F16)
        gv_h = sb("gv_h", [P, CK, GP], F16)
        gv_l = sb("gv_l", [P, CK, GP], F16)
        iota = sb("iota_sb", [4, TK], F32)
        tok_i = sb("tok_i", [4, 3, 2, 2], I32)
        tok_f = sb("tok_f", [4, 3, 4, 2], F32)
        bias_h = sb("bias_h", [4, TQ], F16)
        tok_row = sb("tok_row", [4, TK], F16)

        pt_w = [pt[:, r].rearrange("p (h k q) -> p h k q", h=2, q=TQ) for r in range(2)]
        pt_g = [pt[:, r].rearrange("p (h k q) -> p h k q", h=REP, q=HALF) for r in range(2)]
        g_k_cur, g_k_next = kk[:, 0, 0, :], kk[:, 0, 1, :]
        g_qq = [kk[:, 1, r, :].rearrange("p (j q) -> p j q", j=REP) for r in range(2)]
        g_hi = qq[:, 0, 0, :]
        is_own, is_b = inv_rms[0:4, 0:TK], inv_rms[0:4, TK:2 * TK]
        squares = pt[:, 0, 0:CQ * B * TQ].rearrange("p (c t) -> p c t", c=CQ)
        v_rms, y_rms, t_rms = (pt[:, 1, i * B * TQ:(i + 1) * B * TQ] for i in range(3))

        RMS_PARTS = (slice(0, TQ), slice(TQ, B * TQ))

        def gq_of(t):
            return t[:, 0:P].rearrange("p (m d) -> p m d", d=GD)

        def gk_of(t):
            return t[:, P:P + CK * GD].rearrange("p (m d) -> p m d", d=GD)

        def gv_of(t):
            return t[:, P + CK * GD:GCOLS].rearrange("p (m d) -> p m d", d=GD)

        def gq_r(t, quadrant):
            return t[:, :, :, quadrant, 0:GD].rearrange("p c j d -> p (c j) d")

        ps_s = ctx.enter_context(nc.psum_tensor("ps_s", [P, 2, TK], F32))
        ps_t = ctx.enter_context(nc.psum_tensor("ps_t", [P, 2, BANK], F32))
        ps_o = ctx.enter_context(nc.psum_tensor("ps_o", [P, BANK], F32))
        ps_j = ctx.enter_context(nc.psum_tensor("ps_j", [P, BANK], F32))
        ps_rms = ps_s[:].rearrange("p a (b n) -> p (a b) n", n=BANK)

        s_const = sem("s_const")
        s_x = sem("s_x")
        s_init = sem("s_init")
        s_ctx_raw = sem("s_ctx_raw")
        s_ctx = sem("s_ctx")
        s_xs = sem("s_xs")
        s_pool = sem("s_pool")
        s_dve = sem("s_dve")
        s_raw = sem("s_raw")
        s_wh = sem("s_wh")
        s_wl = sem("s_wl")
        s_wo_raw = sem("s_wo_raw")
        s_woh = sem("s_woh")
        s_wol = sem("s_wol")
        s_rows = sem("s_rows")
        s_score = sem("s_score")
        s_max = sem("s_max")
        s_exp = sem("s_exp")
        s_rinv = sem("s_rinv")
        s_norm = sem("s_norm")
        s_tr = sem("s_tr")
        s_ev = sem("s_ev")
        s_pv = sem("s_pv")
        s_oh = sem("s_oh")
        s_ol = sem("s_ol")
        s_kq_mm = sem("s_kq_mm")
        s_kq_hi = sem("s_kq_hi")
        s_kq = sem("s_kq")
        s_v_mm = sem("s_v_mm")
        s_v_ev = sem("s_v_ev")
        s_v = sem("s_v")
        s_out_mm = sem("s_out_mm")
        s_out = sem("s_out")
        g_raw = sem("g_raw")
        g_wh = sem("g_wh")
        g_wl = sem("g_wl")
        g_wx = sem("g_wx")
        g_wo_raw = sem("g_wo_raw")
        g_woh = sem("g_woh")
        g_wol = sem("g_wol")
        g_k_mm = sem("g_k_mm")
        g_k_hi = sem("g_k_hi")
        g_k_new = sem("g_k_new")
        g_k = sem("g_k")
        g_q_mm = sem("g_q_mm")
        g_q_hi = sem("g_q_hi")
        g_q = sem("g_q")
        g_v_mm = sem("g_v_mm")
        g_v_ev = sem("g_v_ev")
        g_v = sem("g_v")
        g_out_mm = sem("g_out_mm")
        g_out = sem("g_out")
        g_zero = sem("g_zero")
        s_sq = sem("s_sq")
        s_ms = sem("s_ms")
        s_ms_sb = sem("s_ms_sb")
        s_rms = sem("s_rms")
        s_inv = sem("s_inv")
        s_done = sem("s_done")

        block = ctx.enter_context(nc.Block())

        def load_step(w, n, q):
            reaches(nc.sync, s_wl, STEPS * w + n)
            for col, name, chunks in ((WQ0, "wq", CQ), (WK0, "wk", CK), (WV0, "wv", CK)):
                nc.sync.dma_start(
                    w_raw[:, col:col + chunks * P].rearrange("p (c n) -> p c n", n=P),
                    a[f"{name}{w}"].rearrange("(c p) n -> p c n", p=P)[:, :, q * P:(q + 1) * P],
                ).then_inc(s_raw, 16)

        def load_step_wo(w, n, q):
            reaches(nc.sync, s_wol, STEPS * w + n)
            nc.sync.dma_start(wo_raw[:], a[f"wo{w}"][q * P:(q + 1) * P, :]).then_inc(s_wo_raw, 16)

        def load_group(n, g):
            reaches(nc.sync, g_wl, n)
            for col, name, width, chunks in ((0, "gwq", REP * GD, CQ), (P, "gwk", GD, CK), (P + 64, "gwv", GD, CK)):
                nc.sync.dma_start(
                    w_raw[:, col:col + chunks * width].rearrange("p (c n) -> p c n", n=width),
                    a[name].rearrange("(c p) n -> p c n", p=P)[:, :, g * width:(g + 1) * width],
                ).then_inc(g_raw, 16)

        def load_group_wo(n, g):
            reaches(nc.sync, g_wol, n)
            for j in range(REP):
                row = (g * REP + j) * GD
                nc.sync.dma_start(wo_raw[j * GP:j * GP + GD, :], a["gwo"][row:row + GD, :]).then_inc(g_wo_raw, 16)

        @block.sync
        def _(sp):
            for dst, name in ((ident[:], "ident"), (flags[:], "flags"), (iota[:], "iota"), (tok_i[:], "tokens"),
                              (is_own[:, 0:TQ], "masks"), (bo[:], "bo"), (norm_w[:], "norm_w")):
                sp.dma_start(dst, a[name]).then_inc(s_const, 16)
            sp.dma_start(x32[:], a["x_t"].rearrange("(c p) t -> p c t", p=P)).then_inc(s_x, 16)
            for layer in range(4):
                if layer != 1:
                    w = WIDE.index(layer)
                    if layer == 2:
                        sp.wait_ge(g_wl, B * GROUPS)
                        sp.wait_ge(g_wol, B * GROUPS)
                    for q in range(PAIRS):
                        load_step(w, q, q)
                        if q >= 3:
                            load_step_wo(w, q - 3, q - 3)
                    with sp.Fori(1, B) as b:
                        for q in range(PAIRS):
                            load_step(w, b * PAIRS + q, q)
                            load_step_wo(w, b * PAIRS + (q - 3), (q - 3) % PAIRS)
                    for q in range(5, PAIRS):
                        load_step_wo(w, STEPS - PAIRS + q, q)
                else:
                    sp.wait_ge(s_wl, STEPS)
                    sp.wait_ge(g_zero, 1)
                    for g in range(GROUPS):
                        load_group(g, g)
                        if g >= 2:
                            load_group_wo(g - 2, g - 2)
                    with sp.Fori(1, B) as b:
                        for g in range(GROUPS):
                            load_group(b * GROUPS + g, g)
                            load_group_wo(b * GROUPS + (g - 2), (g - 2) % GROUPS)
                    for g in range(2, GROUPS):
                        load_group_wo(B * GROUPS - GROUPS + g, g)
            sp.wait_ge(s_out, 2 * STEPS * len(WIDE))
            sp.dma_start(out.rearrange("(c p) t -> p c t", p=P), x32[:]).then_inc(s_done, 16)
            sp.wait_ge(s_done, 16)

        @block.gpsimd
        def _(pool):
            chain = [0]

            def link(ins):
                chain[0] += 1
                ins.then_inc(s_pool, 1)
                pool.wait_ge(s_pool, chain[0])

            def load_ctx(b, half):
                pool.dma_start(ctx_raw[:], a["ctx_t"].rearrange("b (c p) k -> b p c k", p=P)
                               [b, :, :, half * BANK:(half + 1) * BANK]).then_inc(s_ctx_raw, 16)

            def split_ctx(layer, b, half):
                pool.wait_ge(s_ctx_raw, 16 * (8 * layer + 2 * b + half + 1))
                link(nc.gpsimd.tensor_scalar(ctx_h[:, half], ctx_raw[:], 1.0, None, ALU.mult))
                nc.gpsimd.tensor_tensor(ctx_l[:, half], ctx_raw[:], ctx_h[:, half],
                                        ALU.subtract).then_inc(s_ctx, 1)
                n = 8 * layer + 2 * b + half + 1
                if n < 32:
                    pool.wait_ge(s_ctx, n)
                    load_ctx(n % 8 // 2, n % 2)

            def split_x(src):
                link(nc.gpsimd.tensor_scalar(xh[:], src, 1.0, None, ALU.mult))
                return nc.gpsimd.tensor_tensor(xl[:], src, xh[:], ALU.subtract)

            def context(layer, b, between=None):
                for half in range(2):
                    if half == 1 and between:
                        between()
                    if layer == 1:
                        if b == 0:
                            pool.wait_ge(s_v_mm, 2 * STEPS)
                        else:
                            pool.wait_ge(g_v_mm, 2 * GROUPS * b)
                    elif layer == 2 and b == 0:
                        pool.wait_ge(g_v_mm, 2 * B * GROUPS)
                    else:
                        reaches(pool, s_v_mm, 2 * (STEPS * WIDE.index(layer) + b * PAIRS) - 1 + half)
                    split_ctx(layer, b, half)

            def next_context(layer, b, between=None):
                if b + 1 < B:
                    context(layer, b + 1, between)
                elif layer < 3:
                    context(layer + 1, 0)

            def spread_kv(G):
                pool.wait_ge(g_wl, G + 1)
                for src, k, v in ((gw_h, gk_h, gv_h), (gw_l, gk_l, gv_l)):
                    for quadrant in range(4):
                        nc.gpsimd.tensor_copy(k[:, :, quadrant, 0:GD], gk_of(src))
                    last = nc.gpsimd.tensor_copy(v[:, :, 0:GD], gv_of(src))
                last.then_inc(g_wx, 1)

            def spread_q(G):
                if G > 0:
                    pool.wait_ge(g_q_mm, 4 * G)
                pool.wait_ge(g_wl, G + 1)
                for src, dst in ((gw_h, gq_h), (gw_l, gq_l)):
                    for quadrant in range(4):
                        last = nc.gpsimd.tensor_copy(gq_r(dst, quadrant), gq_of(src))
                last.then_inc(g_wx, 1)

            def normed(b):
                pool.wait_ge(s_inv, 1 if b == 0 else 2)
                t = slice(b * TQ, (b + 1) * TQ)
                for c in range(CQ):
                    last = nc.gpsimd.tensor_tensor(xn32[:, c], x32[:, c, t], inv_rms[:, t], ALU.mult)
                link(last)
                for c in range(CQ):
                    last = nc.gpsimd.tensor_scalar(xn32[:, c], xn32[:, c], norm_w[:, c:c + 1], None, ALU.mult)
                link(last)

            load_ctx(0, 0)
            context(0, 0)
            for layer in range(4):
                if layer != 1:
                    w = WIDE.index(layer)
                    for b in range(B):
                        q = b * PAIRS
                        if b > 0:
                            pool.wait_ge(s_kq_mm, 3 * (STEPS * w + q))
                        elif layer == 0:
                            pool.wait_ge(s_x, 16)
                            pool.wait_ge(s_const, 16 * N_CONST)
                        elif layer == 2:
                            pool.wait_ge(g_out, STEPS)
                        else:
                            pool.wait_ge(s_out, 2 * STEPS * w)
                        xb = x32[:, :, b * TQ:(b + 1) * TQ]
                        link(split_x(xb))
                        for c in range(CQ):
                            last = nc.gpsimd.tensor_scalar(xb[:, c], xb[:, c], bo[:, w * CQ + c:w * CQ + c + 1],
                                                           None, ALU.add)
                        last.then_inc(s_xs, 1)
                        for k in range(PAIRS):
                            if k == PAIRS - 1:
                                next_context(layer, b)
                            pool.wait_ge(s_v_ev, 2 * (STEPS * w + q + k + 1))
                            reaches(pool, s_pv, STEPS * layer + q + k - 1)
                            nc.gpsimd.tensor_copy(v32[:, k % 2], v_new[:]).then_inc(s_v, 1)
                else:
                    spread_kv(0)
                    spread_q(0)
                    normed(0)
                    for b in range(B):
                        reaches(pool, g_q_mm, 2 * PAIRS * b)
                        split_x(xn32[:]).then_inc(s_xs, 1)
                        for k in range(GROUPS):
                            G = b * GROUPS + k
                            if k == 1 and b + 1 < B:
                                pool.wait_ge(s_xs, layer * B + b + 1)
                                normed(b + 1)
                            if G + 1 < B * GROUPS:
                                pool.wait_ge(g_v_mm, 2 * (G + 1))
                                spread_kv(G + 1)
                            if k == GROUPS - 1:
                                next_context(layer, b, lambda: spread_q(G + 1))
                            elif G + 1 < B * GROUPS:
                                spread_q(G + 1)
                            pool.wait_ge(g_v_ev, 2 * (G + 1))
                            pool.wait_ge(s_pv, STEPS * layer + 2 * G)
                            nc.gpsimd.tensor_copy(v32[:, 0, :, 0:GP], v_new[:, :, 0:GP]).then_inc(g_v, 1)

        @block.tensor
        def _(pe):
            pe.wait_ge(s_const, 16 * N_CONST)
            pe.wait_ge(s_init, 1)
            MM = nc.tensor.matmul

            def products(dst, pairs):
                n = 3 * len(pairs)
                terms = [t for wh, wl, xh_, xl_ in pairs for t in ((wh, xh_), (wh, xl_), (wl, xh_))]
                for i, (l, r) in enumerate(terms):
                    last = MM(dst, l, r, start=i == 0, stop=i == n - 1)
                return last

            def transposes(m, s):
                pe.wait_ge(s_norm, m + 1)
                for half in range(2):
                    if not (isinstance(m, int) and m == 0 and half == 0):
                        reaches(pe, s_ev, m * 2 - 1 + half)
                    for k in range(4):
                        kt = half * 4 + k
                        last = nc.tensor.transpose(ps_t[:, half, k * P:(k + 1) * P],
                                                   prob[:, s % 4, kt * P:(kt + 1) * P], ident[:])
                    last.then_inc(s_tr, 1)

            def wide(layer):
                w = WIDE.index(layer)
                T0, U0, W0 = STEPS * layer, UNITS * STEPS * layer, STEPS * w

                def project_k(q, r, half):
                    if half == 0:
                        pe.wait_ge(s_wl, q + (W0 + 1))
                    pe.wait_ge(s_ctx, ctx_count(layer, q, half))
                    products(ps_j[:], [(w_h[:, r, WK0 + c * P:WK0 + (c + 1) * P], w_l[:, r, WK0 + c * P:WK0 + (c + 1) * P],
                                        ctx_h[:, half, c], ctx_l[:, half, c]) for c in range(CK)]).then_inc(s_kq_mm, 1)

                def project_v(q, r, half):
                    for k in range(4):
                        kt = slice(k * P, (k + 1) * P)
                        last = products(ps_o[:, kt], [(ctx_h[:, half, c, kt], ctx_l[:, half, c, kt],
                                                       w_h[:, r, WV0 + c * P:WV0 + (c + 1) * P],
                                                       w_l[:, r, WV0 + c * P:WV0 + (c + 1) * P]) for c in range(CK)])
                    last.then_inc(s_v_mm, 1)

                def project_q(q, r):
                    pe.wait_ge(s_xs, xs_count(layer, q))
                    products(ps_j[:], [(w_h[:, r, WQ0 + c * P:WQ0 + (c + 1) * P], w_l[:, r, WQ0 + c * P:WQ0 + (c + 1) * P],
                                        xh[:, c], xl[:, c]) for c in range(CQ)]).then_inc(s_kq_mm, 1)

                def project_out(c):
                    cc = slice(c * P, (c + 1) * P)
                    products(ps_j[:], [(wo_h[:, cc], wo_l[:, cc], o_h[:], o_l[:])]).then_inc(s_out_mm, 1)

                def scores(p, s, par):
                    n = p * UNITS + (U0 + s)
                    reaches(pe, s_exp, n - 1)
                    h, t = s // QT, slice(s % QT * P, (s % QT + 1) * P)
                    for half in range(2):
                        keys = slice(half * BANK, (half + 1) * BANK)
                        MM(ps_s[:, s % 2, keys], qq[:, par, h, t], kk[:, par, h, keys], start=True, stop=False)
                        last = MM(ps_s[:, s % 2, keys], q2[:, par, h, t], k2[:, par, h, keys], start=False, stop=True)
                    last.then_inc(s_score, 1)

                def attend(p, like, kts):
                    par = (like - 1) % 2
                    if kts[0] == 0:
                        pe.wait_ge(s_ev, p * (2 * UNITS) + 2 * U0)
                        pe.wait_ge(s_v, p + W0)
                        reaches(pe, s_ol, p + (T0 - 1))
                        if like < STEPS - 1:
                            pe.wait_ge(s_v_ev, p * 2 + (2 * W0 + 4))
                    for kt in kts:
                        for h in range(2):
                            last = MM(ps_o[h * HD:(h + 1) * HD, :], v32[:, par, kt, h * HD:(h + 1) * HD],
                                      pt_w[par][:, h, kt, :], start=kt == 0, stop=kt == KT - 1)
                    if kts[-1] == KT - 1:
                        last.then_inc(s_pv, 1)

                def out_wait(m):
                    pe.wait_ge(s_ol, m + (T0 + 1))
                    pe.wait_ge(s_wol, m + (W0 + 1))

                if layer == 2:
                    pe.wait_ge(g_out, STEPS)
                elif layer == 3:
                    pe.wait_ge(s_out, 2 * W0)
                project_k(0, 0, 0)
                project_v(0, 0, 0)
                pe.wait_ge(s_kq, 3 * W0 + 1)
                project_k(0, 0, 1)
                pe.wait_ge(s_v_ev, 2 * W0 + 1)
                project_v(0, 0, 1)
                pe.wait_ge(s_kq, 3 * W0 + 2)
                project_q(0, 0)
                pe.wait_ge(s_rows, w + 1)

                def step(p, like, _):
                    par, nxt = like % 2, like < STEPS - 1
                    q, r = p + 1, 1 - par
                    if like == STEPS:
                        for s in range(2):
                            transposes(p * UNITS + (U0 + s - 2), s - 2)
                        for m in (STEPS - 2, STEPS - 1):
                            if m == STEPS - 1:
                                attend(p, like, range(KT))
                            out_wait(m)
                            for c in range(CQ):
                                reaches(pe, s_out, 2 * (W0 + m) + c)
                                project_out(c)
                        return
                    for s in range(UNITS):
                        if s == 0:
                            pe.wait_ge(s_kq, p * 3 + (3 * W0 + 3))
                        scores(p, s, par)
                        if like > 0 or s >= 2:
                            transposes(p * UNITS + (U0 + s - 2), s - 2)
                        if like > 0 and s in PV_AT:
                            attend(p, like, PV_AT[s])
                        if s == 0 and nxt:
                            pe.wait_ge(s_kq, q * 3 + 3 * W0)
                            project_k(q, r, 0)
                        elif s == 1 and nxt:
                            reaches(pe, s_ol, p + (T0 - 1))
                            pe.wait_ge(s_v_ev, q * 2 + 2 * W0)
                            project_v(q, r, 0)
                        elif s == 2 and nxt:
                            pe.wait_ge(s_kq, q * 3 + (3 * W0 + 1))
                            project_k(q, r, 1)
                        elif s == 3 and nxt:
                            pe.wait_ge(s_v_ev, q * 2 + (2 * W0 + 1))
                            project_v(q, r, 1)
                        elif s == 4 and like >= 2:
                            if nxt:
                                pe.wait_ge(s_kq, q * 3 + (3 * W0 + 2))
                            else:
                                pe.wait_ge(s_kq, 3 * (W0 + STEPS))
                            out_wait(p - 2)
                            project_out(0)
                        elif s == 5 and like >= 2:
                            pe.wait_ge(s_out, p * 2 + (2 * W0 - 3))
                            project_out(1)
                        elif s == 6 and nxt:
                            if like >= 2:
                                pe.wait_ge(s_out, p * 2 + (2 * W0 - 2))
                            else:
                                pe.wait_ge(s_kq, q * 3 + (3 * W0 + 2))
                            project_q(q, r)

                run_steps(pe, step)

            def grouped(layer):
                T0, U0 = STEPS * layer, UNITS * STEPS * layer

                for n, batches in enumerate((range(1), range(1, B))):
                    pe.wait_ge(s_sq, n + 1)
                    for b in batches:
                        for c in range(CQ):
                            last = MM(ps_rms[:, b], ones[:], squares[:, c, b * TQ:(b + 1) * TQ], start=c == 0,
                                      stop=c == CQ - 1)
                    last.then_inc(s_ms, 1)

                def project_k(G, half):
                    if half == 0:
                        pe.wait_ge(g_wx, G * 2 + 1)
                    pe.wait_ge(s_ctx, ctx_count(layer, G * 2, half))
                    products(ps_j[:], [(gk_h[:, c], gk_l[:, c], ctx_h[:, half, c], ctx_l[:, half, c])
                                       for c in range(CK)]).then_inc(g_k_mm, 1)

                def project_v(G, half):
                    for k in range(4):
                        kt = slice(k * P, (k + 1) * P)
                        last = products(ps_j[:, k * GP:(k + 1) * GP],
                                        [(ctx_h[:, half, c, kt], ctx_l[:, half, c, kt], gv_h[:, c], gv_l[:, c])
                                         for c in range(CK)])
                    last.then_inc(g_v_mm, 1)

                def project_q(q, qpar, two):
                    pe.wait_ge(s_xs, xs_count(layer, q))
                    rows = slice(qpar * HALF, (qpar + 1) * HALF)
                    for j in (0, 1):
                        last = products(ps_j[:, j * HALF:(j + 1) * HALF],
                                        [(gq_h[:, c, 2 * two + j], gq_l[:, c, 2 * two + j], xh[:, c, rows], xl[:, c, rows])
                                         for c in range(CQ)])
                    last.then_inc(g_q_mm, 1)

                def project_out():
                    for c in range(CQ):
                        cc = slice(c * P, (c + 1) * P)
                        last = products(ps_j[:, c * HALF:(c + 1) * HALF],
                                        [(wo_h[:, cc], wo_l[:, cc], o_h[:, 0:HALF], o_l[:, 0:HALF])])
                    last.then_inc(g_out_mm, 1)

                def out_wait(m, G):
                    pe.wait_ge(s_ol, m + (T0 + 1))
                    pe.wait_ge(g_wol, G)

                def scores(p, s, par):
                    n = p * UNITS + (U0 + s)
                    reaches(pe, s_exp, n - 1)
                    for half in range(2):
                        keys = slice(half * BANK, (half + 1) * BANK)
                        last = MM(ps_s[:, s % 2, keys], g_qq[par][:, s // 2, s % 2 * P:(s % 2 + 1) * P],
                                  g_k_cur[:, keys], start=True, stop=True)
                    last.then_inc(s_score, 1)

                def attend(p, like, G, kts):
                    par = (like - 1) % 2
                    if kts[0] == 0:
                        pe.wait_ge(s_ev, p * (2 * UNITS) + 2 * U0)
                        pe.wait_ge(g_v, G)
                        reaches(pe, s_ol, p + (T0 - 1))
                    for kt in kts:
                        for j in range(REP):
                            last = MM(ps_o[j * GP:(j + 1) * GP, 0:HALF], v32[:, 0, kt, 0:GP],
                                      pt_g[par][:, j, kt, :], start=kt == 0, stop=kt == KT - 1)
                    if kts[-1] == KT - 1:
                        last.then_inc(s_pv, 1)

                pe.wait_ge(s_out, 2 * STEPS)
                project_k(0, 0)
                pe.wait_ge(g_k_new, 1)
                project_k(0, 1)
                pe.wait_ge(g_k_new, 2)
                pe.wait_ge(g_wx, 2)
                project_q(0, 0, 0)
                pe.wait_ge(g_q, 1)
                project_q(0, 0, 1)

                def step(p, like, G):
                    par, nxt, knxt = like % 2, like < STEPS - 1, like < STEPS - 2
                    q = p + 1
                    if like == STEPS:
                        for s in range(2):
                            transposes(p * UNITS + (U0 + s - 2), s - 2)
                        for m in (STEPS - 2, STEPS - 1):
                            if m == STEPS - 1:
                                attend(p, like, G, range(KT))
                            out_wait(m, B * GROUPS)
                            pe.wait_ge(g_out, m)
                            project_out()
                        return
                    for s in range(UNITS):
                        if s == 0:
                            pe.wait_ge(g_q, p * 2 + 2)
                            if par == 0:
                                pe.wait_ge(g_k, G + 1)
                        scores(p, s, par)
                        if like > 0 or s >= 2:
                            transposes(p * UNITS + (U0 + s - 2), s - 2)
                        if like > 0 and s in PV_AT:
                            attend(p, like, G if par == 0 else G + 1, PV_AT[s])
                        if par == 0:
                            if s == 0:
                                pe.wait_ge(g_q, p * 2 + 2)
                                project_v(G, 0)
                            elif s == 1:
                                pe.wait_ge(g_v_ev, G * 2 + 1)
                                project_v(G, 1)
                            elif s == 2 and like >= 2:
                                pe.wait_ge(g_v_ev, G * 2 + 2)
                                out_wait(p - 2, G)
                                project_out()
                            elif s == 4 and nxt:
                                if like >= 2:
                                    pe.wait_ge(g_out, p - 1)
                                else:
                                    pe.wait_ge(g_v_ev, G * 2 + 2)
                                project_q(q, 1, 0)
                            elif s == 6 and nxt:
                                pe.wait_ge(g_q, q * 2 + 1)
                                project_q(q, 1, 1)
                        else:
                            if s == 1 and like >= 2:
                                pe.wait_ge(g_q, p * 2 + 2)
                                out_wait(p - 2, G)
                                project_out()
                            elif s == 2 and knxt:
                                if like >= 2:
                                    pe.wait_ge(g_out, p - 1)
                                else:
                                    pe.wait_ge(g_q, p * 2 + 2)
                                project_k(G + 1, 0)
                            elif s == 3 and knxt:
                                pe.wait_ge(g_k_new, G * 2 + 3)
                                project_k(G + 1, 1)
                            elif s == 4 and nxt:
                                pe.wait_ge(g_k_new, G * 2 + 4)
                                pe.wait_ge(g_wx, G * 2 + 4)
                                project_q(q, 0, 0)
                            elif s == 6 and nxt:
                                pe.wait_ge(g_q, q * 2 + 1)
                                project_q(q, 0, 1)

                run_steps(pe, step)

            for layer in range(4):
                grouped(layer) if layer == 1 else wide(layer)

        @block.scalar
        def _(act):
            A = nc.scalar.activation
            act.wait_ge(s_const, 16 * N_CONST)
            act.wait_ge(s_init, 1)

            def exponentials(n, s):
                act.wait_ge(s_max, n + 1)
                A(prob[:, s % 4, :], ps_s[:, s % 2, :], ACT.Exp, bias=negmax[:, s % 4:s % 4 + 1],
                  accum_out=rsum[:, s % 4:s % 4 + 1]).then_inc(s_exp, 1)

            def evacuate(m, dst):
                for half in range(2):
                    act.wait_ge(s_tr, m * 2 + (1 + half))
                    A(dst(half), ps_t[:, half, :].rearrange("p (k q) -> p k q", k=4), ACT.Copy).then_inc(s_ev, 1)

            def output_hi(T0, m, n):
                act.wait_ge(s_pv, m + (T0 + 1))
                A(o_h[:, 0:n], ps_o[:, 0:n], ACT.Copy).then_inc(s_oh, 1)

            def wide(layer):
                w = WIDE.index(layer)
                T0, U0, W0 = STEPS * layer, UNITS * STEPS * layer, STEPS * w

                def weights_hi(q, r):
                    act.wait_ge(s_raw, q * 48 + 48 * (W0 + 1))
                    A(w_h[:, r], w_raw[:], ACT.Copy, scale=WS).then_inc(s_wh, 1)

                def wo_hi(m):
                    act.wait_ge(s_wo_raw, m * 16 + 16 * (W0 + 1))
                    A(wo_h[:], wo_raw[:], ACT.Copy, scale=WS).then_inc(s_woh, 1)

                def keys_hi(q, r, half):
                    act.wait_ge(s_kq_mm, q * 3 + (3 * W0 + 1 + half))
                    keys = slice(half * BANK, (half + 1) * BANK)
                    A(k2[0:HD, r, 0, keys], ps_j[0:HD, :], ACT.Copy, scale=1 / WS)
                    A(k2[HD:P, r, 1, keys], ps_j[HD:P, :], ACT.Copy, scale=1 / WS).then_inc(s_kq_hi, 1)

                def queries_hi(q, r):
                    act.wait_ge(s_kq_mm, q * 3 + (3 * W0 + 3))
                    A(qq[0:HD, r, 0, :], ps_j[0:HD, :], ACT.Copy, scale=QS)
                    A(qq[HD:P, r, 1, :], ps_j[HD:P, :], ACT.Copy, scale=QS).then_inc(s_kq_hi, 1)

                def values(q, half):
                    act.wait_ge(s_v_mm, q * 2 + (2 * W0 + 1 + half))
                    if half == 0:
                        reaches(act, s_v, q + W0)
                    A(v_new[:, half * 4:half * 4 + 4, :], ps_o[:].rearrange("p (k d) -> p k d", k=4), ACT.Copy,
                      scale=VS / WS).then_inc(s_v_ev, 1)

                weights_hi(0, 0)
                keys_hi(0, 0, 0)
                values(0, 0)
                keys_hi(0, 0, 1)
                values(0, 1)
                weights_hi(1, 1)
                queries_hi(0, 0)

                def step(p, like, _):
                    par, nxt = like % 2, like < STEPS - 1
                    q, r = p + 1, 1 - par

                    def pt_half(s):
                        u, side = (s - 2) % UNITS, (par if s >= 2 else 1 - par)
                        rows = slice(u % QT * P, (u % QT + 1) * P)
                        return lambda half: pt_w[side][:, u // QT, half * 4:half * 4 + 4, rows]

                    if like == STEPS:
                        output_hi(T0, p - 2, TQ)
                        wo_hi(p - 2)
                        for s in range(2):
                            evacuate(p * UNITS + (U0 + s - 2), pt_half(s))
                        act.wait_ge(s_out_mm, 2 * (W0 + STEPS - 1))
                        wo_hi(p - 1)
                        output_hi(T0, p - 1, TQ)
                        return
                    for s in range(UNITS):
                        if s == 0 and like >= 2:
                            output_hi(T0, p - 2, TQ)
                        if s == 1 and like >= 2:
                            wo_hi(p - 2)
                        if nxt:
                            if s in (1, 3):
                                keys_hi(q, r, s // 2)
                            elif s in (2, 4):
                                values(q, s // 2 - 1)
                            elif s == 7:
                                queries_hi(q, r)
                        if like > 0 or s >= 2:
                            if s == 2 and like >= 2:
                                act.wait_ge(s_pv, p + (T0 - 1))
                            evacuate(p * UNITS + (U0 + s - 2), pt_half(s))
                        exponentials(p * UNITS + (U0 + s), s)
                        if s == 6 and like < STEPS - 2:
                            weights_hi(p + 2, par)

                run_steps(act, step)

            def grouped(layer):
                T0, U0 = STEPS * layer, UNITS * STEPS * layer

                def weights_hi(G):
                    act.wait_ge(g_raw, G * 48 + 48)
                    if not isinstance(G, int) or G > 0:
                        act.wait_ge(g_wx, G * 2)
                    A(gw_h[:], w_raw[:, 0:GCOLS], ACT.Copy, scale=WS).then_inc(g_wh, 1)

                def wo_hi(G):
                    act.wait_ge(g_wo_raw, G * 64 + 64)
                    A(wo_h[:], wo_raw[:], ACT.Copy, scale=WS).then_inc(g_woh, 1)

                weights_hi(0)
                for n, t in enumerate(RMS_PARTS):
                    act.wait_ge(s_ms_sb, n + 1)
                    A(y_rms[:, t], v_rms[:, t], ACT.Ln).then_inc(s_rms, 1)
                    act.wait_ge(s_rms, 2 * n + 1)
                    A(y_rms[:, t], y_rms[:, t], ACT.Exp, scale=-0.5).then_inc(s_rms, 1)

                def part(sem_mm, count, flag, sem_hi):
                    act.wait_ge(sem_mm, count)
                    A(g_hi, ps_j[:], ACT.Copy, scale=flags[:, flag:flag + 1]).then_inc(sem_hi, 1)

                def values(G, half):
                    act.wait_ge(g_v_mm, G * 2 + (1 + half))
                    if half == 0:
                        if isinstance(G, int) and G == 0:
                            act.wait_ge(s_v, STEPS)
                        else:
                            act.wait_ge(g_v, G)
                    A(v_new[:, half * 4:half * 4 + 4, 0:GP], ps_j[:, 0:4 * GP].rearrange("p (k d) -> p k d", k=4),
                      ACT.Copy, scale=VS / WS).then_inc(g_v_ev, 1)

                part(g_k_mm, 1, FLAG_K, g_k_hi)
                part(g_k_mm, 2, FLAG_K, g_k_hi)
                part(g_q_mm, 1, FLAG_Q, g_q_hi)
                part(g_q_mm, 2, FLAG_Q, g_q_hi)

                def step(p, like, G):
                    par, nxt, knxt = like % 2, like < STEPS - 1, like < STEPS - 2
                    q = p + 1

                    def pt_half(s):
                        u, side = (s - 2) % UNITS, (par if s >= 2 else 1 - par)
                        rows = slice(u % 2 * P, (u % 2 + 1) * P)
                        return lambda half: pt_g[side][:, u // 2, half * 4:half * 4 + 4, rows]

                    if like == STEPS:
                        act.wait_ge(g_out_mm, STEPS - 2)
                        output_hi(T0, p - 2, HALF)
                        wo_hi(G - 1)
                        for s in range(2):
                            evacuate(p * UNITS + (U0 + s - 2), pt_half(s))
                        act.wait_ge(g_out_mm, STEPS - 1)
                        output_hi(T0, p - 1, HALF)
                        return
                    for s in range(UNITS):
                        if s == 0 and like >= 2:
                            output_hi(T0, p - 2, HALF)
                        if s == 1 and like >= 2 and par == 0:
                            wo_hi(G - 1)
                        if par == 0 and s in (1, 2):
                            values(G, s - 1)
                        if par == 1 and s in (3, 4) and knxt:
                            part(g_k_mm, G * 2 + s, FLAG_K, g_k_hi)
                        if s in (5, 7) and nxt:
                            part(g_q_mm, q * 2 + (1 if s == 5 else 2), FLAG_Q, g_q_hi)
                        if like > 0 or s >= 2:
                            if s == 2 and like >= 2:
                                act.wait_ge(s_pv, p + (T0 - 1))
                            evacuate(p * UNITS + (U0 + s - 2), pt_half(s))
                        exponentials(p * UNITS + (U0 + s), s)
                        if s == 2 and par == 0 and like < STEPS - 2:
                            weights_hi(G + 1)

                run_steps(act, step)

            for layer in range(4):
                grouped(layer) if layer == 1 else wide(layer)

        @block.vector
        def _(dve):
            V = nc.vector
            chain = [0]

            def link(ins):
                chain[0] += 1
                ins.then_inc(s_dve, 1)
                dve.wait_ge(s_dve, chain[0])

            def split_lo(dst, src, scale, hi):
                return V.scalar_tensor_tensor(dst, src, scale, hi, ALU.mult, ALU.subtract)

            for t in (k2, q2, gq_h, gq_l, gk_h, gk_l, gv_h, gv_l):
                V.memset(t[:], 0.0)
            link(V.memset(ones[:], 1.0 / C))
            dve.wait_ge(s_const, 16 * N_CONST)
            link(V.tensor_scalar(is_b[:, 0:TQ], is_own[:, 0:TQ], -1.0, 1.0, ALU.mult, ALU.add))
            link(V.tensor_scalar(is_b[:, 0:TQ], is_b[:, 0:TQ], -SUPPRESS, None, ALU.mult))
            link(V.tensor_copy(bias_h[:], is_b[:, 0:TQ]))
            link(V.tensor_scalar(is_own[:, 0:TQ], bias_h[:], flags[0:4, FLAG_LO:FLAG_LO + 1], None, ALU.mult))
            link(V.tensor_tensor(bias_h[:], is_b[:, 0:TQ], is_own[:, 0:TQ], ALU.subtract))
            for par in range(2):
                V.tensor_copy(q2[HD:HD + 4, par, 0, :], bias_h[:])
                V.tensor_copy(q2[0:4, par, 1, :], bias_h[:])
            for i in range(3):
                V.tensor_copy(tok_f[:, i, 0:2, :], tok_i[:, i])
                last = V.tensor_scalar(tok_f[:, i, 2:4, :], tok_i[:, i], float(TK), None, ALU.add)
            last.then_inc(s_init, 1)
            dve.wait_ge(s_init, 1)

            def maximum(n, s):
                dve.wait_ge(s_score, n + 1)
                V.tensor_reduce(negmax[:, s % 4:s % 4 + 1], ps_s[:, s % 2, :], AX_X, ALU.max,
                                negate=True).then_inc(s_max, 1)

            def normalize(n, s):
                k = s % 4
                dve.wait_ge(s_exp, n + 1)
                V.reciprocal(rinv[:, k:k + 1], rsum[:, k:k + 1]).then_inc(s_rinv, 1)
                dve.wait_ge(s_rinv, n + 1)
                V.tensor_scalar(prob[:, k, :], prob[:, k, :], rinv[:, k:k + 1], None, ALU.mult).then_inc(s_norm, 1)

            def token_rows(w, pieces):
                for i in pieces:
                    if i < 8:
                        dst, side, j = (is_own, is_b)[i // 4], i // 4, i % 4
                        t = tok_f[:, w, side + 2 * (j // 2), j % 2:j % 2 + 1]
                        if j == 0:
                            link(V.tensor_scalar(dst, iota[:], t, None, ALU.is_equal))
                        else:
                            link(V.scalar_tensor_tensor(dst, iota[:], t, dst, ALU.is_equal, ALU.max))
                    elif i == 8:
                        link(V.scalar_tensor_tensor(is_b, is_b, flags[0:4, FLAG_A:FLAG_A + 1], is_own, ALU.mult,
                                                    ALU.mult))
                    else:
                        link(V.tensor_tensor(tok_row[:], is_own, is_b, ALU.subtract))

            def next_rows(w, like, s):
                piece = (like - (STEPS - 2)) * UNITS + s
                if 0 <= piece < 10 and like < STEPS:
                    token_rows(w, [piece])

            def output_lo(T0, m, n):
                dve.wait_ge(s_oh, m + (T0 + 1))
                V.tensor_tensor(o_l[:, 0:n], ps_o[:, 0:n], o_h[:, 0:n], ALU.subtract).then_inc(s_ol, 1)

            def wide(layer):
                w = WIDE.index(layer)
                T0, U0, W0 = STEPS * layer, UNITS * STEPS * layer, STEPS * w

                def weights_lo(q, r):
                    dve.wait_ge(s_wh, q + (W0 + 1))
                    split_lo(w_l[:, r], w_raw[:], WS, w_h[:, r]).then_inc(s_wl, 1)

                def wo_lo(m):
                    dve.wait_ge(s_woh, m + (W0 + 1))
                    split_lo(wo_l[:], wo_raw[:], WS, wo_h[:]).then_inc(s_wol, 1)

                def keys_lo(q, r, half):
                    dve.wait_ge(s_kq_hi, q * 3 + (3 * W0 + 1 + half))
                    keys = slice(half * BANK, (half + 1) * BANK)
                    split_lo(kk[HD:P, r, 0, keys], ps_j[0:HD, :], 1 / WS, k2[0:HD, r, 0, keys])
                    split_lo(kk[0:HD, r, 1, keys], ps_j[HD:P, :], 1 / WS, k2[HD:P, r, 1, keys])
                    V.tensor_copy(kk[0:HD, r, 0, keys], k2[0:HD, r, 0, keys])
                    V.tensor_copy(kk[HD:P, r, 1, keys], k2[HD:P, r, 1, keys]).then_inc(s_kq, 1)

                def queries_lo(q, r):
                    dve.wait_ge(s_kq_hi, q * 3 + (3 * W0 + 3))
                    split_lo(q2[0:HD, r, 0, :], ps_j[0:HD, :], QS, qq[0:HD, r, 0, :])
                    split_lo(q2[HD:P, r, 1, :], ps_j[HD:P, :], QS, qq[HD:P, r, 1, :])
                    V.tensor_copy(qq[HD:P, r, 0, :], qq[0:HD, r, 0, :])
                    V.tensor_copy(qq[0:HD, r, 1, :], qq[HD:P, r, 1, :]).then_inc(s_kq, 1)

                def add_out(m, c, batch):
                    dve.wait_ge(s_out_mm, m * 2 + (2 * W0 + 1 + c))
                    xs = x32[:, c, bass.ds(batch * TQ, TQ)]
                    V.scalar_tensor_tensor(xs, ps_j[:], 1 / (WS * VS), xs, ALU.mult, ALU.add).then_inc(s_out, 1)

                if w == 0:
                    token_rows(0, range(5))
                weights_lo(0, 0)
                if w == 0:
                    token_rows(0, range(5, 10))
                for par in range(2):
                    V.tensor_copy(k2[HD:HD + 4, par, 0, :], tok_row[:])
                    last = V.tensor_copy(k2[0:4, par, 1, :], tok_row[:])
                last.then_inc(s_rows, 1)
                keys_lo(0, 0, 0)
                keys_lo(0, 0, 1)
                weights_lo(1, 1)
                queries_lo(0, 0)

                def step(p, like, _):
                    par, nxt = like % 2, like < STEPS - 1
                    q, r = p + 1, 1 - par
                    bat = batch_of(p - 2)
                    if like == STEPS:
                        normalize(p * UNITS + (U0 - 1), -1)
                        output_lo(T0, p - 2, TQ)
                        wo_lo(p - 2)
                        add_out(p - 2, 0, bat)
                        add_out(p - 2, 1, bat)
                        wo_lo(p - 1)
                        output_lo(T0, p - 1, TQ)
                        add_out(p - 1, 0, bat)
                        add_out(p - 1, 1, bat)
                        return
                    for s in range(UNITS):
                        if s == 0 and like >= 2:
                            output_lo(T0, p - 2, TQ)
                        if s == 2 and like >= 2:
                            wo_lo(p - 2)
                        if nxt and s in (1, 3):
                            keys_lo(q, r, s // 2)
                        elif like >= 2 and s in (5, 6):
                            add_out(p - 2, s - 5, bat)
                        elif nxt and s == 7:
                            queries_lo(q, r)
                        maximum(p * UNITS + (U0 + s), s)
                        if like > 0 or s > 0:
                            normalize(p * UNITS + (U0 + s - 1), s - 1)
                        if layer == 2:
                            next_rows(2, like, s)
                        if s == 7 and like < STEPS - 2:
                            weights_lo(p + 2, par)

                run_steps(dve, step)

            def grouped(layer):
                T0, U0 = STEPS * layer, UNITS * STEPS * layer

                V.memset(wo_raw[:], 0.0).then_inc(g_zero, 1)
                def weights_lo(G):
                    dve.wait_ge(g_wh, G + 1)
                    split_lo(gw_l[:], w_raw[:, 0:GCOLS], WS, gw_h[:]).then_inc(g_wl, 1)

                def wo_lo(G):
                    dve.wait_ge(g_woh, G + 1)
                    split_lo(wo_l[:], wo_raw[:], WS, wo_h[:]).then_inc(g_wol, 1)

                dve.wait_ge(s_out, 2 * STEPS)
                for t in RMS_PARTS:
                    for c in range(CQ):
                        last = V.tensor_tensor(squares[:, c, t], x32[:, c, t], x32[:, c, t], ALU.mult)
                    last.then_inc(s_sq, 1)
                weights_lo(0)

                def mean_square(n, t):
                    dve.wait_ge(s_ms, n + 1)
                    V.tensor_scalar(v_rms[:, t], ps_s[:].rearrange("p a b -> p (a b)")[:, t], EPS, None,
                                    ALU.add).then_inc(s_ms_sb, 1)

                def newton(n, t):
                    dve.wait_ge(s_rms, 2 * n + 2)
                    link(V.tensor_tensor(t_rms[:, t], y_rms[:, t], y_rms[:, t], ALU.mult))
                    link(V.tensor_tensor(t_rms[:, t], t_rms[:, t], v_rms[:, t], ALU.mult))
                    link(V.tensor_scalar(t_rms[:, t], t_rms[:, t], -0.5, 1.5, ALU.mult, ALU.add))
                    V.tensor_tensor(inv_rms[:, t], t_rms[:, t], y_rms[:, t], ALU.mult).then_inc(s_inv, 1)

                mean_square(0, RMS_PARTS[0])
                newton(0, RMS_PARTS[0])
                mean_square(1, RMS_PARTS[1])
                newton(1, RMS_PARTS[1])

                def keys(n, half):
                    dve.wait_ge(g_k_hi, n)
                    split_lo(g_k_next[:, half * BANK:(half + 1) * BANK], ps_j[:], 1 / WS, g_hi).then_inc(g_k_new, 1)

                def queries(n, par, two):
                    dve.wait_ge(g_q_hi, n)
                    split_lo(g_qq[par][:, 2 * two:2 * two + 2, :].rearrange("p a b -> p (a b)"), ps_j[:], GQS,
                             g_hi).then_inc(g_q, 1)

                def keys_in_place(G):
                    dve.wait_ge(g_k_new, G * 2 + 2)
                    V.tensor_copy(g_k_cur, g_k_next).then_inc(g_k, 1)

                def add_out(m, half, batch):
                    dve.wait_ge(g_out_mm, m + 1)
                    xs = x32[:, :, bass.ds(batch * TQ + half * HALF, HALF)]
                    V.scalar_tensor_tensor(xs, ps_j[:].rearrange("p (c q) -> p c q", c=CQ), 1 / (WS * VS), xs,
                                           ALU.mult, ALU.add).then_inc(g_out, 1)

                keys(1, 0)
                keys(2, 1)
                queries(1, 0, 0)
                queries(2, 0, 1)

                def step(p, like, G):
                    par, nxt, knxt = like % 2, like < STEPS - 1, like < STEPS - 2
                    q = p + 1
                    bat = batch_of(p - 2)
                    if like == STEPS:
                        normalize(p * UNITS + (U0 - 1), -1)
                        output_lo(T0, p - 2, HALF)
                        wo_lo(G - 1)
                        add_out(p - 2, 0, bat)
                        output_lo(T0, p - 1, HALF)
                        add_out(p - 1, 1, bat)
                        return
                    for s in range(UNITS):
                        if s == 0 and par == 0:
                            keys_in_place(G)
                        if s == 0 and like >= 2:
                            output_lo(T0, p - 2, HALF)
                        if s == 1 and like >= 2 and par == 0:
                            wo_lo(G - 1)
                        if like >= 2 and s == (3 if par == 0 else 2):
                            add_out(p - 2, par, bat)
                        if par == 1 and s in (3, 4) and knxt:
                            keys(G * 2 + s, s - 3)
                        if s in (5, 7) and nxt:
                            queries(q * 2 + (1 if s == 5 else 2), 1 - par, s // 7)
                        maximum(p * UNITS + (U0 + s), s)
                        if like > 0 or s > 0:
                            normalize(p * UNITS + (U0 + s - 1), s - 1)
                        next_rows(1, like, s)
                        if s == 3 and par == 0 and like < STEPS - 2:
                            weights_lo(G + 1)

                run_steps(dve, step)

            for layer in range(4):
                grouped(layer) if layer == 1 else wide(layer)


def constants(np):
    flags = np.zeros((P, 4), np.float32)
    rows = np.arange(P)
    flags[:, FLAG_Q] = GQS * (rows // GP % 2 == 1)
    flags[:, FLAG_K] = (rows // GP >= 2) / WS
    flags[:, FLAG_LO] = rows % 2 == 1
    flags[:, FLAG_A] = rows < 2
    iota = np.tile(np.arange(TK, dtype=np.float32), (4, 1))
    return {"ident": np.eye(P, dtype=np.float32), "flags": flags, "iota": iota}


def kernel(**inputs):
    import numpy as np
    import concourse.bacc as bacc
    from concourse.bass_utils import run_bass_kernel_spmd

    def get(name):
        return np.ascontiguousarray(inputs[name])

    arrays = constants(np)
    arrays["x_t"] = np.ascontiguousarray(get("x").reshape(B * TQ, C).T)
    arrays["ctx_t"] = np.ascontiguousarray(get("ctx_2048").transpose(0, 2, 1))
    mask_a, mask_b = get("mask_S_fk1"), get("mask_S_fk0")
    arrays["masks"] = np.stack([mask_a, mask_a, mask_b, mask_b])
    for i, layer in enumerate(WIDE):
        for name in ("Wq", "Wk", "Wv", "Wo"):
            arrays[f"{name.lower()}{i}"] = get(f"L{layer}_xattn_{name}")
    tok = [(get(f"L{layer}_xattn_token_indices_A"), get(f"L{layer}_xattn_token_indices_B")) for layer in WIDE]
    arrays["tokens"] = np.stack([np.stack([np.stack([t[row // 2], t[1]]) for t in tok]) for row in range(4)])
    arrays["bo"] = np.ascontiguousarray(
        np.stack([get(f"L{layer}_xattn_bo") for layer in WIDE]).reshape(len(WIDE) * CQ, P).T)
    for name in ("wq", "wk", "wv", "wo"):
        arrays[f"g{name}"] = get(f"L1_xattn_{name}")
    arrays["norm_w"] = np.ascontiguousarray(get("L1_xattn_norm_w").reshape(CQ, P).T)

    nc = bacc.Bacc("TRN2", target_bir_lowering=False, num_devices=1)
    a = {k: nc.dram_tensor(k, v.shape, mybir.dt.from_np(v.dtype), kind="ExternalInput").ap()
         for k, v in arrays.items()}
    out = nc.dram_tensor("out_t", (C, B * TQ), F32, kind="ExternalOutput").ap()
    build(nc, a, out)
    got = run_bass_kernel_spmd(nc, [arrays], core_ids=[0]).results[0]["out_t"]
    return np.ascontiguousarray(got.T).reshape(B, TQ, C)
```
